# Optimizing a Trainium2 kernel written in Bass

```python
import numpy as np
import jax
import jax.numpy as jnp

def _softmax(x, axis=-1):
    return jax.nn.softmax(x, axis=axis)

def _gelu(x):
    return jax.nn.gelu(x, approximate=True)

def _silu(x):
    return jax.nn.silu(x)

def _sigmoid(x):
    return jax.nn.sigmoid(x)

def _layernorm(x, axis=-1, eps=1e-05):
    m = jnp.mean(x, axis=axis, keepdims=True)
    v = jnp.var(x, axis=axis, keepdims=True)
    return (x - m) / jnp.sqrt(v + eps)

def _scatter_add(tgt, idx, src, axis=0):
    return tgt.at[idx].add(src)

def _segment_sum(src, seg, n):
    return jax.ops.segment_sum(src, seg, n)
kernel_name = 'mk_seq_postln_d1_jaxref_r8_d81b5e'

def setup_inputs(seed: int=0):
    np.random.seed(seed)
    _w = jnp.asarray

    def _L0_attn_setup():
        import jax, jax.numpy as jnp
        import numpy as np
        D_MODEL = 128
        D_STATE = 128
        BATCH = 8
        SEQ = 512
        key = jax.random.key(seed)
        ks = jax.random.split(key, 10)
        s = 0.1
        return {'x': jax.random.normal(ks[0], (BATCH, SEQ, D_MODEL), dtype=jnp.float32), 'Wi': jax.random.normal(ks[1], (D_STATE, D_MODEL), dtype=jnp.float32) * 0.02, 'bi': jnp.zeros((D_STATE,), dtype=jnp.float32), 'Ws': jax.random.normal(ks[2], (D_STATE, D_MODEL), dtype=jnp.float32) * 0.02, 'bs': jnp.zeros((D_STATE,), dtype=jnp.float32), 'Wo': jax.random.normal(ks[3], (D_MODEL, D_STATE), dtype=jnp.float32) * 0.02, 'bo': jnp.zeros((D_MODEL,), dtype=jnp.float32), 'A': jax.random.normal(ks[4], (D_STATE, D_STATE), dtype=jnp.float32) * s, 'B': jax.random.normal(ks[5], (D_STATE, D_STATE), dtype=jnp.float32) * s, 'C': jax.random.normal(ks[6], (D_STATE, D_STATE), dtype=jnp.float32) * s}
    _L0_attn_in = _L0_attn_setup()

    def _L0_ffn_setup():
        import jax, jax.numpy as jnp
        import numpy as np
        DIM = 128
        HIDDEN = 384
        SCALE = 1.0 / 127.0

        def _dequant(w_int, dtype):
            return w_int.astype(dtype) * jnp.asarray(SCALE, dtype)
        key = jax.random.key(seed)
        k_x, k_g, k_u, k_d = jax.random.split(key, 4)
        x = jax.random.normal(k_x, (4, 256, DIM), dtype=jnp.float32)
        w_gate = jax.random.randint(k_g, (HIDDEN, DIM), -127, 128, dtype=jnp.int32)
        w_up = jax.random.randint(k_u, (HIDDEN, DIM), -127, 128, dtype=jnp.int32)
        w_down = jax.random.randint(k_d, (DIM, HIDDEN), -127, 128, dtype=jnp.int32)
        return {'x': x, 'w_gate': w_gate, 'w_up': w_up, 'w_down': w_down}
    _L0_ffn_in = _L0_ffn_setup()
    _d = {'L0_attn_x': _L0_attn_in['x'], 'L0_attn_Wi': _L0_attn_in['Wi'], 'L0_attn_bi': _L0_attn_in['bi'], 'L0_attn_Ws': _L0_attn_in['Ws'], 'L0_attn_bs': _L0_attn_in['bs'], 'L0_attn_Wo': _L0_attn_in['Wo'], 'L0_attn_bo': _L0_attn_in['bo'], 'L0_attn_A': _L0_attn_in['A'], 'L0_attn_B': _L0_attn_in['B'], 'L0_attn_C': _L0_attn_in['C'], 'L0_ffn_w_gate': _L0_ffn_in['w_gate'], 'L0_ffn_w_up': _L0_ffn_in['w_up'], 'L0_ffn_w_down': _L0_ffn_in['w_down']}
    _x0 = _d['L0_attn_x']
    _d['L0_attn_x'] = jax.random.normal(jax.random.fold_in(jax.random.key(seed), 1), (8, 512, 128), dtype=_x0.dtype)
    del _x0
    return _d

def reference(L0_attn_x, L0_attn_Wi, L0_attn_bi, L0_attn_Ws, L0_attn_bs, L0_attn_Wo, L0_attn_bo, L0_attn_A, L0_attn_B, L0_attn_C, L0_ffn_w_gate, L0_ffn_w_up, L0_ffn_w_down):

    def _L0_attn_ref(x, Wi, bi, Ws, bs, Wo, bo, A, B, C):
        import jax, jax.numpy as jnp
        import numpy as np
        D_MODEL = 128
        D_STATE = 128
        BATCH = 8
        SEQ = 512
        u = jnp.einsum('bsd,nd->bsn', x, Wi) + bi
        sp = jnp.einsum('bsd,nd->bsn', x, Ws) + bs

        def step(state, inp):
            u_t, sp_t = inp
            state = jnp.tanh(state @ A.T + u_t @ B.T) + sp_t
            y_t = state @ C.T
            return (state, y_t)
        state0 = jnp.zeros((x.shape[0], A.shape[0]), dtype=x.dtype)
        _, ys = jax.lax.scan(step, state0, (u.transpose(1, 0, 2), sp.transpose(1, 0, 2)))
        ys = ys.transpose(1, 0, 2)
        out = jnp.einsum('bsn,dn->bsd', ys, Wo) + bo
        return out

    def _L0_ffn_ref(x, w_gate, w_up, w_down):
        import jax, jax.numpy as jnp
        import numpy as np
        DIM = 128
        HIDDEN = 384
        SCALE = 1.0 / 127.0

        def _dequant(w_int, dtype):
            return w_int.astype(dtype) * jnp.asarray(SCALE, dtype)
        wg = _dequant(w_gate, x.dtype)
        wu = _dequant(w_up, x.dtype)
        wd = _dequant(w_down, x.dtype)
        gate = jnp.einsum('bsd,hd->bsh', x, wg)
        up = jnp.einsum('bsd,hd->bsh', x, wu)
        h = jax.nn.silu(gate) * up
        return jnp.einsum('bsh,dh->bsd', h, wd)
    x = L0_attn_x
    x = _layernorm(x + _L0_attn_ref(x, L0_attn_Wi, L0_attn_bi, L0_attn_Ws, L0_attn_bs, L0_attn_Wo, L0_attn_bo, L0_attn_A, L0_attn_B, L0_attn_C), axis=-1)
    x = _layernorm(x + _L0_ffn_ref(x, L0_ffn_w_gate, L0_ffn_w_up, L0_ffn_w_down), axis=-1)
    return x

_drawn_inputs = setup_inputs


def setup_inputs(seed=0):
    import zlib

    import numpy as np

    out = dict(_drawn_inputs(seed))
    spreads = {'L0_attn_bi': (0.0, 0.1), 'L0_attn_bs': (0.0, 0.1), 'L0_attn_bo': (0.0, 0.1)}
    factors = {}
    for name, (base, spread) in spreads.items():
        noise = np.random.default_rng([zlib.crc32(name.encode()), seed]).standard_normal(out[name].shape)
        drawn = base * np.exp(spread * noise) if base else spread * noise
        out[name] = jnp.asarray(drawn.astype(out[name].dtype))
    for name, factor in factors.items():
        out[name] = (out[name] * factor).astype(out[name].dtype)
    return out
```

```python
import concourse.bass as bass
from concourse import mybir
from contextlib import ExitStack

BATCH, SEQ, D, HIDDEN = 8, 512, 128, 384
STEPS = 16
BLK = STEPS * BATCH
NBLK = SEQ // STEPS
HT = HIDDEN // D
EPS = 1e-5
SCALE = 1.0 / 127.0
RSQRT_MAGIC = 0x5F3759DF - 0x40000000 - 0x00400000
NEWTON = 3
X_CHUNKS = [(0, 256), (256, 1024), (1024, 4096)]


def post_ln_recurrent_block(nc, x_t, w_chain, w_out, bo_row, w_gate_up, w_down, out):
    fp32, int32 = mybir.dt.float32, mybir.dt.int32
    ALU = mybir.AluOpType
    TANH = mybir.ActivationFunctionType.Tanh

    ctx = ExitStack()
    with ctx:
        def sb(name, shape, dt=fp32):
            return ctx.enter_context(nc.sbuf_tensor(name, shape, dt))

        def bank(name):
            return ctx.enter_context(nc.psum_tensor(name, [128, 512], fp32))

        def sem(name):
            return ctx.enter_context(nc.semaphore(name))

        x_sb = sb("x_sb", [D, SEQ * BATCH])
        wc = sb("wc", [D, 4 * D + 2])
        A_T, B_T, Wi, Ws = (wc[:, i * D:(i + 1) * D] for i in range(4))
        bs_col, bi_col = wc[:, 4 * D:4 * D + 1], wc[:, 4 * D + 1:4 * D + 2]
        wo = sb("wo", [D, 2 * D])
        C, Wo_T = wo[:, 0:D], wo[:, D:2 * D]
        bo_sb = sb("bo_sb", [1, D])
        wgu_int = sb("wgu_int", [D, 2 * HIDDEN], int32)
        wd_int = sb("wd_int", [D, HT * D], int32)
        wgu = sb("wgu", [D, 2 * HIDDEN])
        wd = sb("wd", [D, HT * D])
        prev_x_T = sb("prev_x_T", [D, 2 * D])
        AWs_T, BWi_T = prev_x_T[:, 0:D], prev_x_T[:, D:2 * D]
        WoC_T = sb("WoC_T", [D, D])
        mix_x_T = sb("mix_x_T", [D, D])
        bias_rows = sb("bias_rows", [1, 3 * D])
        Abs_row, Bbi_row, z_bias = (bias_rows[0:1, i * D:(i + 1) * D] for i in range(3))
        out_bias = sb("out_bias", [BLK, D])
        bs_wide = sb("bs_wide", [D, BLK])
        ones = sb("ones", [128, BLK])
        ident = sb("ident", [128, 128])
        x_blk = sb("x_blk", [D, 2, BLK])
        h = sb("h", [D, 2, BLK])
        v1 = sb("v1", [BLK, D])
        x1 = sb("x1", [BLK, 2, D])
        x1_T = sb("x1_T", [D, BLK])
        th = sb("th", [D, HT, BLK])
        gt = sb("gt", [D, HT, BLK])
        hid = sb("hid", [D, HT, BLK])
        v2 = sb("v2", [BLK, D])
        y = sb("y", [BLK, 2, D])
        stats = sb("stats", [BLK, 2, 6])
        mv = sb("mv", [BLK, 2, 2])
        rs = sb("rs", [BLK, 2, 3])

        pre = [bank("pre_even"), bank("pre_odd")]
        mix_ps, x1T_ps, gate_ps, up_ps, down_ps = (
            bank(n) for n in ("mix_ps", "x1T_ps", "gate_ps", "up_ps", "down_ps"))
        setup_ps = bank("setup_ps")

        wc_loaded, wo_loaded, ffn_loaded = sem("wc_loaded"), sem("wo_loaded"), sem("ffn_loaded")
        x_loaded = [sem(f"x_loaded{i}") for i in range(len(X_CHUNKS))]
        consts_ready = sem("consts_ready")
        products = sem("products")
        folded = sem("folded")
        weights_ready = sem("weights_ready")
        x_blk_ready = sem("x_blk_ready")
        x_blk_used = sem("x_blk_used")
        z_ready = sem("z_ready")
        h_ready = sem("h_ready")
        mix_ready, mix_taken = sem("mix_ready"), sem("mix_taken")
        x1_ready = sem("x1_ready")
        x1T_ready, x1T_copied = sem("x1T_ready"), sem("x1T_copied")
        gate_ready, up_ready = sem("gate_ready"), sem("up_ready")
        th_ready = sem("th_ready")
        hid_ready = sem("hid_ready")
        down_ready, down_taken = sem("down_ready"), sem("down_taken")
        y_ready = sem("y_ready")
        y_stored = [sem("y_stored_even"), sem("y_stored_odd")]
        dve_step = sem("dve_step")

        LAST = NBLK - 1
        block = ctx.enter_context(nc.Block())

        @block.sync
        def _(sp):
            sp.dma_start(wc[:], w_chain[:, :]).then_inc(wc_loaded, 16)
            for i in (1, 2):
                a, b = X_CHUNKS[i]
                sp.dma_start(x_sb[:, a:b], x_t[:, a:b]).then_inc(x_loaded[i], 16)

            def store(k, parity):
                sp.wait_ge(y_ready, k + 1)
                sp.dma_start(out[bass.ds(k * BLK, BLK), :], y[:, parity, :]).then_inc(y_stored[parity], 16)

            with nc.sync.Fori(0, NBLK // 2) as j:
                store(j * 2, 0)
                store(j * 2 + 1, 1)
            for parity in range(2):
                sp.wait_ge(y_stored[parity], 16 * (NBLK // 2))

        @block.gpsimd
        def _(pool):
            nc.gpsimd.memset(ones[:], 1.0).then_inc(consts_ready, 1)
            pool.wait_ge(consts_ready, 1)
            nc.gpsimd.affine_select(out=ident[:], in_=ones[:], compare_op=ALU.is_equal, fill=0.0,
                                    base=0, pattern=[[-1, 128]],
                                    channel_multiplier=1).then_inc(consts_ready, 1)

            def copy_x(k, parity, first=False):
                if not first:
                    pool.wait_ge(x_blk_used, k - 1)
                nc.gpsimd.tensor_copy(x_blk[:, parity, :],
                                      x_sb[:, bass.ds(k * BLK, BLK)]).then_inc(x_blk_ready, 1)

            pool.wait_ge(x_loaded[0], 16)
            copy_x(0, 0, first=True)
            copy_x(1, 1, first=True)
            pool.wait_ge(x_loaded[1], 16)
            pool.wait_ge(x_loaded[2], 16)
            with nc.gpsimd.Fori(1, NBLK // 2) as j:
                copy_x(j * 2, 0)
                copy_x(j * 2 + 1, 1)

        @block.scalar
        def _(act):
            a, b = X_CHUNKS[0]
            act.dma_start(x_sb[:, a:b], x_t[:, a:b]).then_inc(x_loaded[0], 16)
            act.dma_start(wo[:], w_out[:, :]).then_inc(wo_loaded, 16)
            act.dma_start(bo_sb[:], bo_row[:, :]).then_inc(wo_loaded, 16)
            act.dma_start(wgu_int[:], w_gate_up[:, :]).then_inc(ffn_loaded, 16)
            act.dma_start(wd_int[:], w_down[:, :]).then_inc(ffn_loaded, 16)

            def chain_tanh(k, i, parity):
                act.wait_ge(z_ready, k * STEPS + i + 1)
                nc.scalar.activation(h[:, parity, i * BATCH:(i + 1) * BATCH],
                                     pre[parity][:, i * BATCH:(i + 1) * BATCH],
                                     TANH).then_inc(h_ready, 1)

            def gate_tanh(k, j):
                act.wait_ge(gate_ready, k + 1)
                nc.scalar.activation(th[:, j, :], gate_ps[:, j * BLK:(j + 1) * BLK], TANH,
                                     scale=0.5).then_inc(th_ready, 1)

            def period(k, parity, ffn=True):
                for i in range(STEPS):
                    chain_tanh(k, i, parity)
                    if ffn and 11 <= i < 11 + HT:
                        gate_tanh(k - 1, i - 11)

            period(0, 0, ffn=False)
            period(1, 1)
            with nc.scalar.Fori(1, NBLK // 2 - 1) as j:
                period(j * 2, 0)
                period(j * 2 + 1, 1)
            period(LAST - 1, 0)
            period(LAST, 1)
            for j in range(HT):
                gate_tanh(LAST, j)

        @block.tensor
        def _(pe):
            mm = nc.tensor.matmul

            def chain_step(k, i, parity):
                at = i * BATCH
                rhs = h[:, parity, at - BATCH:at] if i else h[:, 1 - parity, BLK - BATCH:BLK]
                pe.wait_ge(h_ready, k * STEPS + i)
                mm(pre[parity][:, at:at + BATCH], A_T, rhs, start=False, stop=True,
                   skip_group_check=True).then_inc(z_ready, 1)

            def pre_x(k, parity):
                mm(pre[parity][:, 0:BLK], BWi_T, x_sb[:, bass.ds(k * BLK, BLK)],
                   start=True, stop=False, skip_group_check=True)

            def pre_prev_x(k, parity):
                mm(pre[parity][:, 0:BLK], AWs_T, x_sb[:, bass.ds(k * BLK - BATCH, BLK)],
                   start=False, stop=False, skip_group_check=True)

            def pre_bias(parity):
                mm(pre[parity][:, 0:BLK], z_bias, ones[0:1, :], start=False, stop=True,
                   skip_group_check=True)

            def mix_x(k, parity, first=False):
                if not first:
                    pe.wait_ge(mix_taken, k)
                pe.wait_ge(x_blk_ready, k + 1)
                mm(mix_ps[:, 0:D], x_blk[:, parity, :], mix_x_T[:], start=True,
                   stop=False).then_inc(x_blk_used, 1)

            def mix_h(parity):
                mm(mix_ps[:, 0:D], h[:, parity, :], WoC_T[:], start=False,
                   stop=True).then_inc(mix_ready, 1)

            def transpose_x1(k, parity):
                pe.wait_ge(x1_ready, k + 1)
                nc.tensor.transpose(x1T_ps[:, 0:BLK], x1[:, parity, :],
                                    ident[:]).then_inc(x1T_ready, 1)

            def gate(k, j):
                pe.wait_ge(x1T_copied, k + 1)
                last = mm(gate_ps[:, j * BLK:(j + 1) * BLK], wgu[:, j * D:(j + 1) * D], x1_T[:],
                          start=True, stop=True)
                if j == HT - 1:
                    last.then_inc(gate_ready, 1)

            def up(j):
                last = mm(up_ps[:, j * BLK:(j + 1) * BLK], wgu[:, HIDDEN + j * D:HIDDEN + (j + 1) * D],
                          x1_T[:], start=True, stop=True)
                if j == HT - 1:
                    last.then_inc(up_ready, 1)

            def down(k, j, first):
                if j == 0:
                    pe.wait_ge(hid_ready, k + 1)
                    if not first:
                        pe.wait_ge(down_taken, k)
                last = mm(down_ps[:, 0:D], hid[:, j, :], wd[:, j * D:(j + 1) * D],
                          start=(j == 0), stop=(j == HT - 1))
                if j == HT - 1:
                    last.then_inc(down_ready, 1)

            def period(k, parity, chain=True, mix=True, ffn_down=2, nxt=True):
                for i in range(STEPS):
                    if not (isinstance(k, int) and k == 0 and i == 0):
                        chain_step(k, i, parity)
                    if i == 0 and mix:
                        mix_h(1 - parity)
                    if 1 <= i <= HT and ffn_down:
                        down(k - 2, i - 1, ffn_down == 1)
                    if nxt and i == 4:
                        pre_x(k + 1, 1 - parity)
                    if nxt and i == 5:
                        pre_prev_x(k + 1, 1 - parity)
                    if nxt and i == 6:
                        pre_bias(1 - parity)
                    if mix and i == 7:
                        transpose_x1(k - 1, 1 - parity)
                    if mix and 8 <= i < 8 + HT:
                        gate(k - 1, i - 8)
                    if mix and 11 <= i < 11 + HT:
                        up(i - 11)
                    if i == STEPS - 1 and not (isinstance(k, int) and k == 0):
                        mix_x(k, parity)

            pe.wait_ge(wc_loaded, 16)
            mm(setup_ps[:, 0:D], Wi, B_T, start=True, stop=True)
            mm(setup_ps[:, D:2 * D], Ws, A_T, start=True, stop=True).then_inc(products, 1)
            mm(mix_ps[0:1, 0:D], bs_col, A_T, start=True, stop=True)
            mm(mix_ps[0:1, D:2 * D], bi_col, B_T, start=True, stop=True).then_inc(products, 1)
            pe.wait_ge(folded, 1)
            pe.wait_ge(x_loaded[0], 16)
            mm(pre[0][:, 0:BLK], BWi_T, x_sb[:, 0:BLK], start=True, stop=False, skip_group_check=True)
            mm(pre[0][:, BATCH:BLK], AWs_T, x_sb[:, 0:BLK - BATCH], start=False, stop=False,
               skip_group_check=True)
            pe.wait_ge(folded, 3)
            pe.wait_ge(consts_ready, 2)
            mm(pre[0][:, BATCH:BLK], Abs_row, ones[0:1, 0:BLK - BATCH], start=False, stop=False,
               skip_group_check=True)
            mm(pre[0][:, 0:BLK], Bbi_row, ones[0:1, :], start=False, stop=True,
               skip_group_check=True).then_inc(z_ready, 1)
            chain_step(0, 1, 0)
            pe.wait_ge(wo_loaded, 32)
            mm(gate_ps[:, 0:D], C, Wo_T, start=True, stop=True).then_inc(products, 1)
            chain_step(0, 2, 0)
            chain_step(0, 3, 0)
            pe.wait_ge(folded, 4)
            mm(up_ps[:, 0:D], Ws, WoC_T[:], start=True, stop=True).then_inc(products, 1)
            chain_step(0, 4, 0)
            pre_x(1, 1)
            chain_step(0, 5, 0)
            pre_prev_x(1, 1)
            chain_step(0, 6, 0)
            pre_bias(1)
            chain_step(0, 7, 0)
            pe.wait_ge(folded, 5)
            mm(down_ps[:, 0:D], bs_wide[:], WoC_T[:], start=True, stop=False)
            chain_step(0, 8, 0)
            mm(down_ps[:, 0:D], ones[0:1, :], bo_sb[:], start=False, stop=True).then_inc(products, 1)
            for i in range(9, STEPS):
                chain_step(0, i, 0)
            pe.wait_ge(folded, 7)
            mix_x(0, 0, first=True)

            pe.wait_ge(x_loaded[1], 16)
            pe.wait_ge(x_loaded[2], 16)
            pe.wait_ge(weights_ready, 2)
            period(1, 1, ffn_down=0)
            period(2, 0, ffn_down=1)
            period(3, 1)
            with nc.tensor.Fori(2, NBLK // 2 - 1) as j:
                period(j * 2, 0)
                period(j * 2 + 1, 1)
            period(LAST - 1, 0)
            period(LAST, 1, nxt=False)
            pe.wait_ge(h_ready, SEQ)
            mix_h(1)
            for j in range(HT):
                down(LAST - 1, j, False)
            transpose_x1(LAST, 1)
            for j in range(HT):
                gate(LAST, j)
            for j in range(HT):
                up(j)
            for j in range(HT):
                down(LAST, j, False)

        @block.vector
        def _(dve):
            class Counter:
                at = 0

            def steps(base):
                Counter.at = base

            def then(ins):
                Counter.at = Counter.at + 1
                ins.then_inc(dve_step, 1)
                dve.wait_ge(dve_step, Counter.at)

            def layernorm(dst, v, n, done):
                then(nc.vector.bn_stats(stats[:, n, :], v))
                nc.vector.nop(nofuse=True)
                then(nc.vector.bn_aggr(mv[:, n, :], stats[:, n, :]))
                mean, var = mv[:, n, 0:1], mv[:, n, 1:2]
                nh, r, t = rs[:, n, 0:1], rs[:, n, 1:2], rs[:, n, 2:3]
                then(nc.vector.tensor_scalar(nh, var, EPS, -0.5, ALU.add, ALU.mult))
                then(nc.vector.tensor_scalar(r.bitcast(int32), nh.bitcast(int32), -0.5,
                                             float(RSQRT_MAGIC), ALU.mult, ALU.add))
                for _ in range(NEWTON):
                    then(nc.vector.tensor_scalar(t, r, r, nh, ALU.mult, ALU.mult))
                    then(nc.vector.tensor_scalar(r, t, 1.5, r, ALU.add, ALU.mult))
                nc.vector.tensor_scalar(dst, v, mean, r, ALU.subtract, ALU.mult).then_inc(done, 1)

            LN_OPS = 4 + 2 * NEWTON

            def norm1(k, parity):
                dve.wait_ge(mix_ready, k + 1)
                nc.vector.tensor_tensor(v1[:], mix_ps[:, 0:D], out_bias[:], ALU.add).then_inc(mix_taken, 1)
                dve.wait_ge(mix_taken, k + 1)
                layernorm(x1[:, parity, :], v1[:], 0, x1_ready)

            def copy_x1T(k):
                dve.wait_ge(x1T_ready, k + 1)
                nc.vector.tensor_copy(x1_T[:], x1T_ps[:, 0:BLK]).then_inc(x1T_copied, 1)

            def hidden(k):
                dve.wait_ge(th_ready, HT * (k + 1))
                then(nc.vector.scalar_tensor_tensor(out=gt[:], in0=th[:], scalar=1.0,
                                                    in1=gate_ps[:, 0:HT * BLK].rearrange("p (j n) -> p j n", j=HT),
                                                    op0=ALU.add, op1=ALU.mult))
                dve.wait_ge(up_ready, k + 1)
                nc.vector.tensor_tensor(hid[:], gt[:], up_ps[:, 0:HT * BLK].rearrange("p (j n) -> p j n", j=HT),
                                        ALU.mult).then_inc(hid_ready, 1)

            def norm2(k, parity, stored=None):
                dve.wait_ge(down_ready, k + 1)
                nc.vector.tensor_tensor(v2[:], down_ps[:, 0:D], x1[:, parity, :], ALU.add).then_inc(down_taken, 1)
                dve.wait_ge(down_taken, k + 1)
                if stored is not None:
                    dve.wait_ge(y_stored[parity], stored * 16)
                layernorm(y[:, parity, :], v2[:], 1, y_ready)

            dve.wait_ge(products, 1)
            nc.vector.tensor_copy(prev_x_T[:, D:2 * D], setup_ps[:, 0:D])
            nc.vector.tensor_copy(prev_x_T[:, 0:D], setup_ps[:, D:2 * D]).then_inc(folded, 1)
            dve.wait_ge(products, 2)
            nc.vector.tensor_copy(bias_rows[0:1, 0:2 * D], mix_ps[0:1, 0:2 * D]).then_inc(folded, 1)
            dve.wait_ge(folded, 2)
            nc.vector.tensor_tensor(z_bias, Abs_row, Bbi_row, ALU.add).then_inc(folded, 1)
            dve.wait_ge(products, 3)
            nc.vector.tensor_copy(WoC_T[:], gate_ps[:, 0:D]).then_inc(folded, 1)
            dve.wait_ge(consts_ready, 2)
            nc.vector.tensor_scalar(bs_wide[:], ones[:], bs_col, None, ALU.mult).then_inc(folded, 1)
            dve.wait_ge(products, 4)
            nc.vector.tensor_tensor(mix_x_T[:], ident[:], up_ps[:, 0:D], ALU.add).then_inc(folded, 1)
            dve.wait_ge(products, 5)
            nc.vector.tensor_copy(out_bias[:], down_ps[:, 0:D]).then_inc(folded, 1)
            dve.wait_ge(folded, 7)
            dve.wait_ge(ffn_loaded, 32)
            nc.vector.tensor_scalar(wgu[:], wgu_int[:], SCALE, None, ALU.mult).then_inc(weights_ready, 1)
            nc.vector.tensor_scalar(wd[:], wd_int[:], SCALE, 0.5, ALU.mult, ALU.mult).then_inc(weights_ready, 1)

            steps(0)
            norm1(0, 0)
            copy_x1T(0)
            hidden(0)
            norm1(1, 1)
            copy_x1T(1)
            norm2(0, 0)
            hidden(1)
            norm1(2, 0)
            copy_x1T(2)
            norm2(1, 1)
            hidden(2)
            done = Counter.at
            per = 2 * LN_OPS + 1

            def period(k, parity, stored):
                norm1(k - 1, 1 - parity)
                copy_x1T(k - 1)
                norm2(k - 2, parity, stored)
                hidden(k - 1)

            with nc.vector.Fori(2, NBLK // 2) as j:
                steps((j - 2) * (2 * per) + done)
                period(j * 2, 0, j - 1)
                period(j * 2 + 1, 1, j - 1)
            steps(done + (NBLK - 4) * per)
            norm1(LAST, 1)
            norm2(LAST - 1, 0, NBLK // 2 - 1)
            copy_x1T(LAST)
            hidden(LAST)
            norm2(LAST, 1, NBLK // 2 - 1)


def kernel(L0_attn_x, L0_attn_Wi, L0_attn_bi, L0_attn_Ws, L0_attn_bs, L0_attn_Wo, L0_attn_bo,
           L0_attn_A, L0_attn_B, L0_attn_C, L0_ffn_w_gate, L0_ffn_w_up, L0_ffn_w_down):
    import numpy as np
    import concourse.bacc as bacc
    from concourse.bass_utils import run_bass_kernel_spmd

    cat = np.concatenate
    arrays = {
        "x_t": np.ascontiguousarray(np.transpose(L0_attn_x, (2, 1, 0))).reshape(D, SEQ * BATCH),
        "w_chain": cat([np.transpose(L0_attn_A), np.transpose(L0_attn_B), L0_attn_Wi, L0_attn_Ws,
                        np.reshape(L0_attn_bs, (D, 1)), np.reshape(L0_attn_bi, (D, 1))], axis=1),
        "w_out": cat([L0_attn_C, np.transpose(L0_attn_Wo)], axis=1),
        "bo_row": np.reshape(L0_attn_bo, (1, D)),
        "w_gate_up": cat([np.transpose(L0_ffn_w_gate), np.transpose(L0_ffn_w_up)], axis=1),
        "w_down": np.transpose(np.reshape(np.transpose(L0_ffn_w_down), (HT, D, D)), (1, 0, 2)).reshape(D, HT * D),
    }
    arrays = {n: np.ascontiguousarray(a) for n, a in arrays.items()}
    nc = bacc.Bacc("TRN2", target_bir_lowering=False, num_devices=1)
    ins = [nc.dram_tensor(n, a.shape, mybir.dt.from_np(a.dtype), kind="ExternalInput").ap()
           for n, a in arrays.items()]
    out = nc.dram_tensor("out", (SEQ * BATCH, D), mybir.dt.float32, kind="ExternalOutput").ap()
    post_ln_recurrent_block(nc, *ins, out)
    r = run_bass_kernel_spmd(nc, [arrays], core_ids=[0])
    rows = r.results[0]["out"]
    return np.ascontiguousarray(np.transpose(np.reshape(rows, (SEQ, BATCH, D)), (1, 0, 2)))
```

```python
import concourse.bass as bass
from concourse import mybir
from contextlib import ExitStack

BATCH, SEQ, D, HIDDEN = 8, 512, 128, 384
STEPS = 16
BLK = STEPS * BATCH
NBLK = SEQ // STEPS
HT = HIDDEN // D
EPS = 1e-5
SCALE = 1.0 / 127.0
RSQRT_MAGIC = 0x5F3759DF - 0x40000000 - 0x00400000
NEWTON = 3
X_CHUNKS = [(0, 2 * BLK), (2 * BLK, SEQ * BATCH)]
TAIL_WARM = 8
WARM = 448


def post_ln_recurrent_block(nc, x_t, w_chain, w_out, bo_row, w_gate_up, w_down, out):
    fp32, int32 = mybir.dt.float32, mybir.dt.int32
    ALU = mybir.AluOpType
    TANH = mybir.ActivationFunctionType.Tanh

    ctx = ExitStack()
    with ctx:
        def sb(name, shape, dt=fp32):
            return ctx.enter_context(nc.sbuf_tensor(name, shape, dt))

        def bank(name):
            return ctx.enter_context(nc.psum_tensor(name, [128, 512], fp32))

        def sem(name):
            return ctx.enter_context(nc.semaphore(name))

        x_sb = sb("x_sb", [D, SEQ * BATCH])
        wc = sb("wc", [D, 4 * D + 2])
        A_T, B_T, Wi, Ws = (wc[:, i * D:(i + 1) * D] for i in range(4))
        bs_col, bi_col = wc[:, 4 * D:4 * D + 1], wc[:, 4 * D + 1:4 * D + 2]
        wo = sb("wo", [D, 2 * D])
        C, Wo_T = wo[:, 0:D], wo[:, D:2 * D]
        bo_sb = sb("bo_sb", [1, D])
        wgu_int = sb("wgu_int", [D, 2 * HIDDEN], int32)
        wd_int = sb("wd_int", [D, HT * D], int32)
        wgu = sb("wgu", [D, 2 * HIDDEN])
        wd = sb("wd", [D, HT * D])
        prev_x_T = sb("prev_x_T", [D, 2 * D])
        AWs_T, BWi_T = prev_x_T[:, 0:D], prev_x_T[:, D:2 * D]
        WoC_T = sb("WoC_T", [D, D])
        mix_x_T = sb("mix_x_T", [D, D])
        z_bias = sb("z_bias", [1, D])
        bs_wide, bi_wide = sb("bs_wide", [D, BLK]), sb("bi_wide", [D, BLK])
        out_bias = sb("out_bias", [1, D])
        warm = sb("warm", [128, 512], mybir.dt.bfloat16)
        ones = sb("ones", [128, BLK])
        ident = sb("ident", [128, 128])
        x_blk = sb("x_blk", [D, 2, BLK])
        h = sb("h", [D, 2, BLK])
        x1 = sb("x1", [BLK, 2, D])
        x1_T = sb("x1_T", [D, BLK])
        th = sb("th", [D, HT, BLK])
        gt = sb("gt", [D, HT, BLK])
        hid = sb("hid", [D, HT, BLK])
        y = sb("y", [BLK, 2, D])
        stats = sb("stats", [BLK, 2, 6])
        mv = sb("mv", [BLK, 2, 2])
        rs = sb("rs", [BLK, 2, 3])

        pre = [bank("pre_even"), bank("pre_odd")]
        mix_ps, x1T_ps, gate_ps, up_ps, down_ps = (
            bank(n) for n in ("mix_ps", "x1T_ps", "gate_ps", "up_ps", "down_ps"))
        warm_ps = bank("warm_ps")

        last_gate = [pre[0], pre[1], gate_ps]
        last_up = [up_ps, x1T_ps, mix_ps]

        wc_loaded, wo_loaded, ffn_loaded = sem("wc_loaded"), sem("wo_loaded"), sem("ffn_loaded")
        x_loaded = [sem(f"x_loaded{i}") for i in range(len(X_CHUNKS))]
        warm_ready = sem("warm_ready")
        consts_ready = sem("consts_ready")
        products = sem("products")
        wide_ready = sem("wide_ready")
        folded = sem("folded")
        weights_ready = sem("weights_ready")
        x_blk_ready = sem("x_blk_ready")
        x_blk_used = sem("x_blk_used")
        z_ready = sem("z_ready")
        h_ready = sem("h_ready")
        mix_ready = sem("mix_ready")
        x1_ready = sem("x1_ready")
        x1T_ready, x1T_copied = sem("x1T_ready"), sem("x1T_copied")
        gate_ready, up_ready = sem("gate_ready"), sem("up_ready")
        th_ready = sem("th_ready")
        hid_ready = sem("hid_ready")
        down_ready = sem("down_ready")
        y_ready = sem("y_ready")
        y_stored = [sem("y_stored_even"), sem("y_stored_odd")]
        dve_step = sem("dve_step")

        LAST = NBLK - 1
        block = ctx.enter_context(nc.Block())

        @block.sync
        def _(sp):
            sp.dma_start(wc[:], w_chain[:, :]).then_inc(wc_loaded, 16)
            sp.dma_start(wo[:], w_out[:, :]).then_inc(wo_loaded, 16)
            sp.dma_start(bo_sb[:], bo_row[:, :]).then_inc(wo_loaded, 16)
            a, b = X_CHUNKS[1]
            sp.dma_start(x_sb[:, a:b], x_t[:, a:b]).then_inc(x_loaded[1], 16)

            def store(k, parity):
                sp.wait_ge(y_ready, k + 1)
                sp.dma_start(out[bass.ds(k * BLK, BLK), :], y[:, parity, :]).then_inc(y_stored[parity], 16)

            with nc.sync.Fori(0, NBLK // 2) as j:
                store(j * 2, 0)
                store(j * 2 + 1, 1)
            for parity in range(2):
                sp.wait_ge(y_stored[parity], 16 * (NBLK // 2))

        @block.gpsimd
        def _(pool):
            nc.gpsimd.memset(ones[:], 1.0).then_inc(consts_ready, 1)
            pool.wait_ge(consts_ready, 1)
            nc.gpsimd.affine_select(out=ident[:], in_=ones[:], compare_op=ALU.is_equal, fill=0.0,
                                    base=0, pattern=[[-1, 128]],
                                    channel_multiplier=1).then_inc(consts_ready, 1)

            def copy_x(k, parity, first=False):
                if not first:
                    pool.wait_ge(x_blk_used, k - 1)
                nc.gpsimd.tensor_copy(x_blk[:, parity, :],
                                      x_sb[:, bass.ds(k * BLK, BLK)]).then_inc(x_blk_ready, 1)

            pool.wait_ge(x_loaded[0], 16)
            copy_x(0, 0, first=True)
            copy_x(1, 1, first=True)
            pool.wait_ge(x_loaded[1], 16)
            with nc.gpsimd.Fori(1, NBLK // 2) as j:
                copy_x(j * 2, 0)
                copy_x(j * 2 + 1, 1)

        @block.scalar
        def _(act):
            a, b = X_CHUNKS[0]
            act.dma_start(x_sb[:, a:b], x_t[:, a:b]).then_inc(x_loaded[0], 16)
            act.dma_start(wgu_int[:], w_gate_up[:, :]).then_inc(ffn_loaded, 16)
            act.dma_start(wd_int[:], w_down[:, :]).then_inc(ffn_loaded, 16)

            def chain_tanh(k, i, parity):
                act.wait_ge(z_ready, k * STEPS + i + 1)
                nc.scalar.activation(h[:, parity, i * BATCH:(i + 1) * BATCH],
                                     pre[parity][:, i * BATCH:(i + 1) * BATCH],
                                     TANH).then_inc(h_ready, 1)

            def gate_tanh(k, j, gate_ps=gate_ps, tile=0):
                act.wait_ge(gate_ready, k + 1 + tile)
                nc.scalar.activation(th[:, j, :], gate_ps[:, j * BLK:(j + 1) * BLK], TANH,
                                     scale=0.5).then_inc(th_ready, 1)

            def period(k, parity, ffn=True):
                for i in range(STEPS):
                    chain_tanh(k, i, parity)
                    if ffn and 12 <= i < 12 + HT:
                        gate_tanh(k - 1, i - 12)

            period(0, 0, ffn=False)
            period(1, 1)
            with nc.scalar.Fori(1, NBLK // 2 - 1) as j:
                period(j * 2, 0)
                period(j * 2 + 1, 1)
            period(LAST - 1, 0)
            period(LAST, 1)
            for j in range(HT):
                gate_tanh(LAST, j, gate_ps=last_gate[j], tile=j)

        @block.tensor
        def _(pe):
            mm = nc.tensor.matmul

            def chain_step(k, i, parity):
                at = i * BATCH
                rhs = h[:, parity, at - BATCH:at] if i else h[:, 1 - parity, BLK - BATCH:BLK]
                pe.wait_ge(h_ready, k * STEPS + i)
                mm(pre[parity][:, at:at + BATCH], A_T, rhs, start=False, stop=True,
                   skip_group_check=True).then_inc(z_ready, 1)

            def pre_x(k, parity):
                mm(pre[parity][:, 0:BLK], BWi_T, x_sb[:, bass.ds(k * BLK, BLK)],
                   start=True, stop=False, skip_group_check=True)

            def pre_prev_x(k, parity):
                mm(pre[parity][:, 0:BLK], AWs_T, x_sb[:, bass.ds(k * BLK - BATCH, BLK)],
                   start=False, stop=False, skip_group_check=True)

            def pre_bias(parity):
                mm(pre[parity][:, 0:BLK], z_bias[:], ones[0:1, :], start=False, stop=True,
                   skip_group_check=True)

            def keep_warm(columns):
                mm(warm_ps[:, 0:columns], warm[:, 0:128], warm[:, 0:columns], start=True, stop=True)

            def mix_bias():
                mm(mix_ps[:, 0:D], ones[0:1, :], out_bias[:], start=True, stop=False)

            def mix_x(k, parity):
                pe.wait_ge(x_blk_ready, k + 1)
                mm(mix_ps[:, 0:D], x_blk[:, parity, :], mix_x_T[:], start=False,
                   stop=False).then_inc(x_blk_used, 1)

            def mix_h(parity):
                mm(mix_ps[:, 0:D], h[:, parity, :], WoC_T[:], start=False,
                   stop=True).then_inc(mix_ready, 1)

            def transpose_x1(k, parity):
                pe.wait_ge(x1_ready, k + 1)
                nc.tensor.transpose(x1T_ps[:, 0:BLK], x1[:, parity, :],
                                    ident[:]).then_inc(x1T_ready, 1)

            def gate(k, j, gate_ps=gate_ps, each=False):
                pe.wait_ge(x1T_copied, k + 1)
                last = mm(gate_ps[:, j * BLK:(j + 1) * BLK], wgu[:, j * D:(j + 1) * D], x1_T[:],
                          start=True, stop=True)
                if each or j == HT - 1:
                    last.then_inc(gate_ready, 1)

            def up(j, up_ps=up_ps, each=False):
                last = mm(up_ps[:, j * BLK:(j + 1) * BLK], wgu[:, HIDDEN + j * D:HIDDEN + (j + 1) * D],
                          x1_T[:], start=True, stop=True)
                if each or j == HT - 1:
                    last.then_inc(up_ready, 1)

            def residual(k, first=False):
                if not first:
                    pe.wait_ge(y_ready, k)
                mm(down_ps[:, 0:D], x1_T[:], ident[:], start=True, stop=False)

            def down(k, j, tile=0):
                pe.wait_ge(hid_ready, k + 1 + tile)
                last = mm(down_ps[:, 0:D], hid[:, j, :], wd[:, j * D:(j + 1) * D],
                          start=False, stop=(j == HT - 1))
                if j == HT - 1:
                    last.then_inc(down_ready, 1)

            def period(k, parity, ffn_down=2, nxt=True):
                for i in range(STEPS):
                    chain_step(k, i, parity)
                    keep_warm(512 if i == 7 else WARM // 2 if i == 8 else WARM)
                    if not ffn_down and 4 <= i < 8:
                        keep_warm(192)
                    if i == 0:
                        mix_h(1 - parity)
                    if i == 1 and nxt:
                        pre_x(k + 1, 1 - parity)
                    if i == 2 and nxt:
                        pre_prev_x(k + 1, 1 - parity)
                    if i == 3 and nxt:
                        pre_bias(1 - parity)
                    if i == 4 and ffn_down:
                        residual(k - 2, first=(ffn_down == 1))
                    if 5 <= i < 5 + HT and ffn_down:
                        down(k - 2, i - 5)
                    if i == 8:
                        transpose_x1(k - 1, 1 - parity)
                        mix_bias()
                    if 9 <= i < 9 + HT:
                        gate(k - 1, i - 9)
                    if 12 <= i < 12 + HT:
                        up(i - 12)
                    if i == STEPS - 1:
                        mix_x(k, parity)

            pe.wait_ge(warm_ready, 1)
            for _ in range(6):
                keep_warm(496)

            pe.wait_ge(wc_loaded, 16)
            mm(gate_ps[:, 0:D], Wi, B_T, start=True, stop=True).then_inc(products, 1)
            mm(up_ps[:, 0:D], Ws, A_T, start=True, stop=True).then_inc(products, 1)
            pe.wait_ge(wide_ready, 2)
            mm(pre[0][:, 0:BLK], B_T, bi_wide[:], start=True, stop=False, skip_group_check=True)
            mm(pre[0][:, BATCH:BLK], A_T, bs_wide[:, 0:BLK - BATCH], start=False, stop=False,
               skip_group_check=True)
            pe.wait_ge(folded, 1)
            pe.wait_ge(x_loaded[0], 16)
            mm(pre[0][:, 0:BLK], BWi_T, x_sb[:, 0:BLK], start=False, stop=False, skip_group_check=True)
            pe.wait_ge(folded, 2)
            mm(pre[0][:, BATCH:BLK], AWs_T, x_sb[:, 0:BLK - BATCH], start=False, stop=True,
               skip_group_check=True).then_inc(z_ready, 1)
            for i in range(1, STEPS):
                chain_step(0, i, 0)
                keep_warm(WARM // 2 if i in (11, 15) else WARM)
                if i in (6, 7, 10, 12, 13, 14):
                    keep_warm(192)
                if i == 1:
                    pre_x(1, 1)
                if i == 2:
                    pre_prev_x(1, 1)
                if i == 3:
                    pe.wait_ge(consts_ready, 2)
                    mm(mix_ps[0:1, 0:D], bs_col, A_T, start=True, stop=False)
                if i == 4:
                    mm(mix_ps[0:1, 0:D], bi_col, B_T, start=False, stop=True).then_inc(products, 1)
                if i == 5:
                    pe.wait_ge(wo_loaded, 32)
                    mm(gate_ps[:, 0:D], C, Wo_T, start=True, stop=True).then_inc(products, 1)
                if i == 8:
                    pe.wait_ge(folded, 3)
                    pre_bias(1)
                if i == 9:
                    pe.wait_ge(folded, 4)
                    mm(up_ps[:, 0:D], Ws, WoC_T[:], start=True, stop=True).then_inc(products, 1)
                if i == 11:
                    mm(down_ps[0:1, 0:D], bs_col, WoC_T[:], start=True, stop=False)
                    mm(down_ps[0:1, 0:D], ones[0:1, 0:1], bo_sb[:], start=False,
                       stop=True).then_inc(products, 1)
            pe.wait_ge(folded, 6)
            mix_bias()
            mix_x(0, 0)

            pe.wait_ge(x_loaded[1], 16)
            pe.wait_ge(weights_ready, 2)
            period(1, 1, ffn_down=0)
            period(2, 0, ffn_down=1)
            period(3, 1)
            with nc.tensor.Fori(2, NBLK // 2 - 1) as j:
                period(j * 2, 0)
                period(j * 2 + 1, 1)
            period(LAST - 1, 0)
            period(LAST, 1, nxt=False)
            pe.wait_ge(h_ready, SEQ)
            mix_h(1)
            keep_warm(512)
            residual(LAST - 1)
            for j in range(HT):
                down(LAST - 1, j)
            for _ in range(TAIL_WARM):
                keep_warm(512)
            transpose_x1(LAST, 1)
            keep_warm(512)
            keep_warm(512)
            for j in range(HT):
                gate(LAST, j, gate_ps=last_gate[j], each=True)
            for j in range(HT):
                up(j, up_ps=last_up[j], each=True)
            keep_warm(512)
            residual(LAST)
            for j in range(HT):
                down(LAST, j, tile=j)

        @block.vector
        def _(dve):
            class Counter:
                at = 0

            def signal(ins):
                Counter.at = Counter.at + 1
                ins.then_inc(dve_step, 1)
                return Counter.at

            def scratch(n):
                return mv[:, n, 0:1], mv[:, n, 1:2], rs[:, n, 0:1], rs[:, n, 1:2], rs[:, n, 2:3]

            def ln_stats(v, n):
                return signal(nc.vector.bn_stats(stats[:, n, :], v))

            def ln_moments(n, before):
                dve.wait_ge(dve_step, before)
                if not isinstance(before, int):
                    nc.vector.nop(nofuse=True)
                return signal(nc.vector.bn_aggr(mv[:, n, :], stats[:, n, :]))

            def ln_half(n, before):
                mean, var, nh, r, t = scratch(n)
                dve.wait_ge(dve_step, before)
                return signal(nc.vector.tensor_scalar(nh, var, EPS, -0.5, ALU.add, ALU.mult))

            def ln_guess(n, before):
                mean, var, nh, r, t = scratch(n)
                dve.wait_ge(dve_step, before)
                return signal(nc.vector.tensor_scalar(r.bitcast(int32), nh.bitcast(int32), -0.5,
                                                      float(RSQRT_MAGIC), ALU.mult, ALU.add))

            def ln_square(n, before):
                mean, var, nh, r, t = scratch(n)
                dve.wait_ge(dve_step, before)
                return signal(nc.vector.scalar_tensor_tensor(out=t, in0=r, scalar=nh, in1=r,
                                                             op0=ALU.mult, op1=ALU.mult))

            def ln_improve(n, before):
                mean, var, nh, r, t = scratch(n)
                dve.wait_ge(dve_step, before)
                return signal(nc.vector.scalar_tensor_tensor(out=r, in0=t, scalar=1.5, in1=r,
                                                             op0=ALU.add, op1=ALU.mult))

            def ln_out(dst, v, n, before, done):
                mean, var, nh, r, t = scratch(n)
                dve.wait_ge(dve_step, before)
                nc.vector.tensor_scalar(dst, v, mean, r, ALU.subtract, ALU.mult).then_inc(done, 1)

            def ln_root(n, at):
                at = ln_guess(n, ln_half(n, ln_moments(n, at)))
                for _ in range(NEWTON):
                    at = ln_improve(n, ln_square(n, at))
                return at

            assert NEWTON == 3
            LN_OPS = 4 + 2 * NEWTON

            def norm1(k, parity):
                dve.wait_ge(mix_ready, k + 1)
                v = mix_ps[:, 0:D]
                ln_out(x1[:, parity, :], v, 0, ln_root(0, ln_stats(v, 0)), x1_ready)

            def copy_x1T(k):
                dve.wait_ge(x1T_ready, k + 1)
                nc.vector.tensor_copy(x1_T[:], x1T_ps[:, 0:BLK]).then_inc(x1T_copied, 1)

            def tiles(ps):
                return ps[:, 0:HT * BLK].rearrange("p (j n) -> p j n", j=HT)

            def hidden(k):
                dve.wait_ge(th_ready, HT * (k + 1))
                gated = signal(nc.vector.scalar_tensor_tensor(
                    out=gt[:], in0=th[:], scalar=1.0, in1=tiles(gate_ps), op0=ALU.add, op1=ALU.mult))
                dve.wait_ge(dve_step, gated)
                dve.wait_ge(up_ready, k + 1)
                nc.vector.tensor_tensor(hid[:], gt[:], tiles(up_ps), ALU.mult).then_inc(hid_ready, 1)

            def last_gated(j):
                dve.wait_ge(th_ready, HT * LAST + j + 1)
                return signal(nc.vector.scalar_tensor_tensor(
                    out=gt[:, j, :], in0=th[:, j, :], scalar=1.0,
                    in1=last_gate[j][:, j * BLK:(j + 1) * BLK], op0=ALU.add, op1=ALU.mult))

            def last_hidden(j, gated):
                dve.wait_ge(dve_step, gated)
                dve.wait_ge(up_ready, LAST + 1 + j)
                nc.vector.tensor_tensor(hid[:, j, :], gt[:, j, :],
                                        last_up[j][:, j * BLK:(j + 1) * BLK],
                                        ALU.mult).then_inc(hid_ready, 1)

            def norm2(k, parity, stored=None):
                dve.wait_ge(down_ready, k + 1)
                v = down_ps[:, 0:D]
                root = ln_root(1, ln_stats(v, 1))
                if stored is not None:
                    dve.wait_ge(y_stored[parity], stored * 16)
                ln_out(y[:, parity, :], v, 1, root, y_ready)

            nc.vector.memset(warm[:], 0.0).then_inc(warm_ready, 1)
            dve.wait_ge(consts_ready, 2)
            dve.wait_ge(wc_loaded, 16)
            nc.vector.tensor_scalar(bi_wide[:], ones[:], bi_col, None, ALU.mult).then_inc(wide_ready, 1)
            nc.vector.tensor_scalar(bs_wide[:], ones[:], bs_col, None, ALU.mult).then_inc(wide_ready, 1)
            dve.wait_ge(products, 1)
            nc.vector.tensor_copy(BWi_T, gate_ps[:, 0:D]).then_inc(folded, 1)
            dve.wait_ge(products, 2)
            nc.vector.tensor_copy(AWs_T, up_ps[:, 0:D]).then_inc(folded, 1)
            dve.wait_ge(products, 3)
            nc.vector.tensor_copy(z_bias[:], mix_ps[0:1, 0:D]).then_inc(folded, 1)
            dve.wait_ge(products, 4)
            nc.vector.tensor_copy(WoC_T[:], gate_ps[:, 0:D]).then_inc(folded, 1)
            dve.wait_ge(products, 5)
            nc.vector.tensor_tensor(mix_x_T[:], ident[:], up_ps[:, 0:D], ALU.add).then_inc(folded, 1)
            dve.wait_ge(products, 6)
            nc.vector.tensor_copy(out_bias[:], down_ps[0:1, 0:D]).then_inc(folded, 1)
            dve.wait_ge(ffn_loaded, 32)
            nc.vector.tensor_scalar(wgu[:], wgu_int[:], SCALE, None, ALU.mult).then_inc(weights_ready, 1)
            nc.vector.tensor_scalar(wd[:], wd_int[:], SCALE, 0.5, ALU.mult, ALU.mult).then_inc(weights_ready, 1)

            norm1(0, 0)
            copy_x1T(0)
            hidden(0)
            norm1(1, 1)
            copy_x1T(1)
            norm2(0, 0)
            hidden(1)
            norm1(2, 0)
            copy_x1T(2)
            norm2(1, 1)
            hidden(2)
            ahead = Counter.at
            per_period = 2 * LN_OPS + 1

            def period(k, parity, stored):
                norm1(k - 1, 1 - parity)
                copy_x1T(k - 1)
                norm2(k - 2, parity, stored)
                hidden(k - 1)

            with nc.vector.Fori(2, NBLK // 2) as j:
                Counter.at = (j - 2) * (2 * per_period) + ahead
                period(j * 2, 0, j - 1)
                period(j * 2 + 1, 1, j - 1)
            Counter.at = ahead + (NBLK - 4) * per_period

            dve.wait_ge(mix_ready, LAST + 1)
            v = mix_ps[:, 0:D]
            first = ln_guess(0, ln_half(0, ln_moments(0, ln_stats(v, 0))))
            first = ln_improve(0, ln_square(0, first))
            first = ln_square(0, first)
            dve.wait_ge(down_ready, LAST)
            w = down_ps[:, 0:D]
            second = ln_stats(w, 1)
            first = ln_improve(0, first)
            second = ln_moments(1, second)
            first = ln_square(0, first)
            second = ln_half(1, second)
            first = ln_improve(0, first)
            second = ln_guess(1, second)
            ln_out(x1[:, 1, :], v, 0, first, x1_ready)
            second = ln_improve(1, ln_square(1, second))
            second = ln_square(1, second)
            copy_x1T(LAST)
            second = ln_improve(1, second)
            second = ln_improve(1, ln_square(1, second))
            dve.wait_ge(y_stored[0], 16 * (NBLK // 2 - 1))
            ln_out(y[:, 0, :], w, 1, second, y_ready)
            gated = [last_gated(0), last_gated(1)]
            last_hidden(0, gated[0])
            gated += [last_gated(2)]
            last_hidden(1, gated[1])
            last_hidden(2, gated[2])
            norm2(LAST, 1, NBLK // 2 - 1)


def kernel(L0_attn_x, L0_attn_Wi, L0_attn_bi, L0_attn_Ws, L0_attn_bs, L0_attn_Wo, L0_attn_bo,
           L0_attn_A, L0_attn_B, L0_attn_C, L0_ffn_w_gate, L0_ffn_w_up, L0_ffn_w_down):
    import numpy as np
    import concourse.bacc as bacc
    from concourse.bass_utils import run_bass_kernel_spmd

    cat = np.concatenate
    arrays = {
        "x_t": np.ascontiguousarray(np.transpose(L0_attn_x, (2, 1, 0))).reshape(D, SEQ * BATCH),
        "w_chain": cat([np.transpose(L0_attn_A), np.transpose(L0_attn_B), L0_attn_Wi, L0_attn_Ws,
                        np.reshape(L0_attn_bs, (D, 1)), np.reshape(L0_attn_bi, (D, 1))], axis=1),
        "w_out": cat([L0_attn_C, np.transpose(L0_attn_Wo)], axis=1),
        "bo_row": np.reshape(L0_attn_bo, (1, D)),
        "w_gate_up": cat([np.transpose(L0_ffn_w_gate), np.transpose(L0_ffn_w_up)], axis=1),
        "w_down": np.transpose(np.reshape(np.transpose(L0_ffn_w_down), (HT, D, D)), (1, 0, 2)).reshape(D, HT * D),
    }
    arrays = {n: np.ascontiguousarray(a) for n, a in arrays.items()}
    nc = bacc.Bacc("TRN2", target_bir_lowering=False, num_devices=1)
    ins = [nc.dram_tensor(n, a.shape, mybir.dt.from_np(a.dtype), kind="ExternalInput").ap()
           for n, a in arrays.items()]
    out = nc.dram_tensor("out", (SEQ * BATCH, D), mybir.dt.float32, kind="ExternalOutput").ap()
    post_ln_recurrent_block(nc, *ins, out)
    r = run_bass_kernel_spmd(nc, [arrays], core_ids=[0])
    rows = r.results[0]["out"]
    return np.ascontiguousarray(np.transpose(np.reshape(rows, (SEQ, BATCH, D)), (1, 0, 2)))
```
